# Optimizing a Trainium2 kernel written in Bass

```python
import numpy as np
import jax
import jax.numpy as jnp

def _softmax(x, axis=-1):
    return jax.nn.softmax(x, axis=axis)

def _gelu(x):
    return jax.nn.gelu(x, approximate=True)

def _silu(x):
    return jax.nn.silu(x)

def _sigmoid(x):
    return jax.nn.sigmoid(x)

def _layernorm(x, axis=-1, eps=1e-05):
    m = jnp.mean(x, axis=axis, keepdims=True)
    v = jnp.var(x, axis=axis, keepdims=True)
    return (x - m) / jnp.sqrt(v + eps)

def _scatter_add(tgt, idx, src, axis=0):
    return tgt.at[idx].add(src)

def _segment_sum(src, seg, n):
    return jax.ops.segment_sum(src, seg, n)
kernel_name = 'mk_decoder_postln_d1_seqx_r2_c4ff7d'

def setup_inputs(seed: int=0):
    np.random.seed(seed)
    _w = jnp.asarray

    def _rec_inputs():
        import jax
        import jax.numpy as jnp
        _rk = jax.random.key(seed)
        x = -0.0003929 + 0.9999 * jax.random.normal(jax.random.fold_in(_rk, 1), (32, 256, 512), jnp.float32)
        _lenS = 256 - jax.random.randint(jax.random.fold_in(_rk, 7), (32,), 0, max(1, 256 // 4) + 1, jnp.int32)
        _lenS2 = 256 - jax.random.randint(jax.random.fold_in(_rk, 8), (32,), 0, max(1, 256 // 4) + 1, jnp.int32)
        _ctx_512P = jax.random.normal(jax.random.fold_in(_rk, 11), (32, 16, 256), jnp.float32)
        _ctx_512c = jax.random.dirichlet(jax.random.fold_in(_rk, 511), 0.3 * jnp.ones((16,), jnp.float32), (32, 256))
        _ctx_512t = jnp.einsum('bsk,bkd->bsd', _ctx_512c, _ctx_512P)
        _ctx_512t = _ctx_512t * jax.lax.rsqrt(jnp.mean(jnp.square(_ctx_512t)) + 1e-12) * 0.953939
        ctx_512 = 4.13588e-05 + 0.999923 * (_ctx_512t + 0.3 * jax.random.normal(jax.random.fold_in(_rk, 611), (32, 256, 256), jnp.float32))
        return (x, ctx_512)
    x, ctx_512 = _rec_inputs()

    def _L0_attn_setup():
        import jax, jax.numpy as jnp
        import numpy as np
        D_MODEL = 512
        N_HEADS = 16
        D_HEAD = D_MODEL // N_HEADS
        BATCH = 2
        SEQ = 1024

        def _evolved_attention(x, Wq, bq, Wk, bk, Wv, bv, Wo, bo, Wt, bt, Wg, bg):
            B, S, D = x.shape
            H, dh = (N_HEADS, D_HEAD)

            def heads(y):
                return y.reshape(B, S, H, dh).transpose(0, 2, 1, 3)
            q = heads(x @ Wq + bq)
            k = heads(x @ Wk + bk)
            v = heads(x @ Wv + bv)
            qn = q / jnp.maximum(jnp.linalg.norm(q, axis=-1, keepdims=True), 1e-12)
            kn = k / jnp.maximum(jnp.linalg.norm(k, axis=-1, keepdims=True), 1e-12)
            scores = jnp.einsum('bhqd,bhkd->bhqk', qn, kn)
            temp = jax.nn.sigmoid(x.mean(axis=1) @ Wt + bt) + 0.5
            scores = scores / temp[:, None, None, :]
            kk = max(1, S // 4)
            vals, idx = jax.lax.top_k(scores, kk)
            w = jax.nn.softmax(vals, axis=-1)
            rows = jnp.arange(B * H * S)[:, None]
            attn = jnp.zeros((B * H * S, S), scores.dtype).at[rows, idx.reshape(-1, kk)].set(w.reshape(-1, kk)).reshape(B, H, S, S)
            out = jnp.einsum('bhqk,bhkd->bhqd', attn, v)
            out = out.transpose(0, 2, 1, 3).reshape(B, S, D)
            out = out @ Wo + bo
            gate = jax.nn.sigmoid(x @ Wg + bg)
            return gate * out + (1.0 - gate) * x
        key = jax.random.key(seed)
        ks = jax.random.split(key, 16)
        s = 0.02
        d = D_MODEL
        return {'x': jax.random.normal(ks[0], (BATCH, SEQ, d), jnp.float32), 'Wq': jax.random.normal(ks[1], (d, d), jnp.float32) * s, 'bq': jnp.zeros((d,), jnp.float32), 'Wk': jax.random.normal(ks[2], (d, d), jnp.float32) * s, 'bk': jnp.zeros((d,), jnp.float32), 'Wv': jax.random.normal(ks[3], (d, d), jnp.float32) * s, 'bv': jnp.zeros((d,), jnp.float32), 'Wo': jax.random.normal(ks[4], (d, d), jnp.float32) * s, 'bo': jnp.zeros((d,), jnp.float32), 'Wt': jax.random.normal(ks[5], (d, 1), jnp.float32) * s, 'bt': jnp.zeros((1,), jnp.float32), 'Wg': jax.random.normal(ks[6], (d, d), jnp.float32) * s, 'bg': jnp.zeros((d,), jnp.float32)}
    _L0_attn_all = _L0_attn_setup()
    _L0_attn_in = {k: v for k, v in _L0_attn_all.items() if k in ('Wq', 'bq', 'Wk', 'bk', 'Wv', 'bv', 'Wo', 'bo', 'Wt', 'bt', 'Wg', 'bg')}
    del _L0_attn_all

    def _L0_xattn_setup():
        import jax, jax.numpy as jnp
        import numpy as np
        B, LQ, LK = (8, 1024, 1024)
        QD, KD, VD = (512, 256, 256)
        key = jax.random.key(seed)
        ks = jax.random.split(key, 9)
        s = 0.02
        return {'query': jax.random.normal(ks[0], (B, LQ, QD), jnp.float32), 'key': jax.random.normal(ks[1], (B, LK, KD), jnp.float32), 'value': jax.random.normal(ks[2], (B, LK, VD), jnp.float32), 'Wq': jax.random.normal(ks[3], (QD, QD), jnp.float32) * s, 'bq': jnp.zeros((QD,), jnp.float32), 'Wk': jax.random.normal(ks[4], (KD, QD), jnp.float32) * s, 'bk': jnp.zeros((QD,), jnp.float32), 'Wv': jax.random.normal(ks[5], (VD, QD), jnp.float32) * s, 'bv': jnp.zeros((QD,), jnp.float32)}
    _L0_xattn_all = _L0_xattn_setup()
    _L0_xattn_in = {k: v for k, v in _L0_xattn_all.items() if k in ('Wq', 'bq', 'Wk', 'bk', 'Wv', 'bv')}
    del _L0_xattn_all

    def _L0_ffn_setup():
        import jax, jax.numpy as jnp
        import numpy as np
        key = jax.random.key(seed)
        k_x, k_W, k_b, k_ids, k_w = jax.random.split(key, 5)
        N_ADAPTERS, D_OUT, D_IN = (32, 512, 512)
        B, S = (2, 1024)
        K = 8
        x = jax.random.normal(k_x, (B, S, D_IN), dtype=jnp.float32)
        W = jax.random.normal(k_W, (N_ADAPTERS, D_OUT, D_IN), dtype=jnp.float32)
        b = jax.random.normal(k_b, (N_ADAPTERS, D_OUT), dtype=jnp.float32)
        ids = jax.random.randint(k_ids, (K,), 0, N_ADAPTERS, dtype=jnp.int64)
        weights = jax.random.uniform(k_w, (K,), dtype=jnp.float32)
        return {'x': x, 'W': W, 'b': b, 'ids': ids, 'weights': weights}
    _L0_ffn_all = _L0_ffn_setup()
    _L0_ffn_in = {k: v for k, v in _L0_ffn_all.items() if k in ('W', 'b', 'ids', 'weights')}
    del _L0_ffn_all
    return {'x': x, 'ctx_512': ctx_512, 'L0_attn_Wq': _L0_attn_in['Wq'], 'L0_attn_bq': _L0_attn_in['bq'], 'L0_attn_Wk': _L0_attn_in['Wk'], 'L0_attn_bk': _L0_attn_in['bk'], 'L0_attn_Wv': _L0_attn_in['Wv'], 'L0_attn_bv': _L0_attn_in['bv'], 'L0_attn_Wo': _L0_attn_in['Wo'], 'L0_attn_bo': _L0_attn_in['bo'], 'L0_attn_Wt': _L0_attn_in['Wt'], 'L0_attn_bt': _L0_attn_in['bt'], 'L0_attn_Wg': _L0_attn_in['Wg'], 'L0_attn_bg': _L0_attn_in['bg'], 'L0_xattn_Wq': _L0_xattn_in['Wq'], 'L0_xattn_bq': _L0_xattn_in['bq'], 'L0_xattn_Wk': _L0_xattn_in['Wk'], 'L0_xattn_bk': _L0_xattn_in['bk'], 'L0_xattn_Wv': _L0_xattn_in['Wv'], 'L0_xattn_bv': _L0_xattn_in['bv'], 'L0_ffn_W': _L0_ffn_in['W'], 'L0_ffn_b': _L0_ffn_in['b'], 'L0_ffn_ids': _L0_ffn_in['ids'], 'L0_ffn_weights': _L0_ffn_in['weights']}

def reference(x, ctx_512, L0_attn_Wq, L0_attn_bq, L0_attn_Wk, L0_attn_bk, L0_attn_Wv, L0_attn_bv, L0_attn_Wo, L0_attn_bo, L0_attn_Wt, L0_attn_bt, L0_attn_Wg, L0_attn_bg, L0_xattn_Wq, L0_xattn_bq, L0_xattn_Wk, L0_xattn_bk, L0_xattn_Wv, L0_xattn_bv, L0_ffn_W, L0_ffn_b, L0_ffn_ids, L0_ffn_weights):
    import jax
    import jax.numpy as jnp

    def _L0_attn_ref(x, Wq, bq, Wk, bk, Wv, bv, Wo, bo, Wt, bt, Wg, bg):
        import jax, jax.numpy as jnp
        import numpy as np
        D_MODEL = 512
        N_HEADS = 16
        D_HEAD = D_MODEL // N_HEADS
        BATCH = 2
        SEQ = 1024

        def _evolved_attention(x, Wq, bq, Wk, bk, Wv, bv, Wo, bo, Wt, bt, Wg, bg):
            B, S, D = x.shape
            H, dh = (N_HEADS, D_HEAD)

            def heads(y):
                return y.reshape(B, S, H, dh).transpose(0, 2, 1, 3)
            q = heads(x @ Wq + bq)
            k = heads(x @ Wk + bk)
            v = heads(x @ Wv + bv)
            qn = q / jnp.maximum(jnp.linalg.norm(q, axis=-1, keepdims=True), 1e-12)
            kn = k / jnp.maximum(jnp.linalg.norm(k, axis=-1, keepdims=True), 1e-12)
            scores = jnp.einsum('bhqd,bhkd->bhqk', qn, kn)
            temp = jax.nn.sigmoid(x.mean(axis=1) @ Wt + bt) + 0.5
            scores = scores / temp[:, None, None, :]
            kk = max(1, S // 4)
            vals, idx = jax.lax.top_k(scores, kk)
            w = jax.nn.softmax(vals, axis=-1)
            rows = jnp.arange(B * H * S)[:, None]
            attn = jnp.zeros((B * H * S, S), scores.dtype).at[rows, idx.reshape(-1, kk)].set(w.reshape(-1, kk)).reshape(B, H, S, S)
            out = jnp.einsum('bhqk,bhkd->bhqd', attn, v)
            out = out.transpose(0, 2, 1, 3).reshape(B, S, D)
            out = out @ Wo + bo
            gate = jax.nn.sigmoid(x @ Wg + bg)
            return gate * out + (1.0 - gate) * x
        return _evolved_attention(x, Wq, bq, Wk, bk, Wv, bv, Wo, bo, Wt, bt, Wg, bg)

    def _L0_xattn_ref(query, key, value, Wq, bq, Wk, bk, Wv, bv):
        import jax, jax.numpy as jnp
        import numpy as np
        B, LQ, LK = (8, 1024, 1024)
        QD, KD, VD = (512, 256, 256)
        q = jnp.einsum('bld,de->ble', query, Wq) + bq
        k = jnp.einsum('bld,de->ble', key, Wk) + bk
        v = jnp.einsum('bld,de->ble', value, Wv) + bv
        scores = jnp.einsum('bqe,bke->bqk', q, k)
        attn = jax.nn.softmax(scores, axis=-1)
        out = jnp.einsum('bqk,bke->bqe', attn, v)
        return out

    def _L0_ffn_ref(x, W, b, ids, weights):
        import jax, jax.numpy as jnp
        import numpy as np
        Wsel = W[ids]
        bsel = b[ids]
        out = jnp.einsum('k,kod,bsd->bso', weights, Wsel, x)
        out = out + jnp.einsum('k,ko->o', weights, bsel)
        return out
    x = _layernorm(x + _L0_attn_ref(x, L0_attn_Wq, L0_attn_bq, L0_attn_Wk, L0_attn_bk, L0_attn_Wv, L0_attn_bv, L0_attn_Wo, L0_attn_bo, L0_attn_Wt, L0_attn_bt, L0_attn_Wg, L0_attn_bg), axis=-1)
    x = _layernorm(x + _L0_xattn_ref(x, ctx_512, ctx_512, L0_xattn_Wq, L0_xattn_bq, L0_xattn_Wk, L0_xattn_bk, L0_xattn_Wv, L0_xattn_bv), axis=-1)
    x = _layernorm(x + _L0_ffn_ref(x, L0_ffn_W, L0_ffn_b, L0_ffn_ids, L0_ffn_weights), axis=-1)
    return x

_drawn_inputs = setup_inputs


def setup_inputs(seed=0):
    import zlib

    import numpy as np

    out = dict(_drawn_inputs(seed))
    spreads = {'L0_attn_bq': (0.0, 0.8),
     'L0_attn_bk': (0.0, 0.8),
     'L0_attn_bv': (0.0, 0.544),
     'L0_attn_bo': (0.0, 0.1),
     'L0_attn_bg': (0.0, 0.508),
     'L0_xattn_bq': (0.0, 0.1),
     'L0_xattn_bk': (0.0, 0.8),
     'L0_xattn_bv': (0.0, 0.1)}
    factors = {'L0_attn_Wq': 6.72,
     'L0_attn_Wk': 6.646,
     'L0_attn_Wv': 5.937,
     'L0_attn_Wo': 3.218,
     'L0_attn_Wt': 8.0}
    for name, (base, spread) in spreads.items():
        noise = np.random.default_rng([zlib.crc32(name.encode()), seed]).standard_normal(out[name].shape)
        drawn = base * np.exp(spread * noise) if base else spread * noise
        out[name] = jnp.asarray(drawn.astype(out[name].dtype))
    for name, factor in factors.items():
        out[name] = (out[name] * factor).astype(out[name].dtype)
    return out
```

```python
from contextlib import ExitStack

import concourse.bass as bass
from concourse import mybir

P = 128
ALU = mybir.AluOpType
ACT = mybir.ActivationFunctionType
AX = mybir.AxisListType
F32 = mybir.dt.float32
BF16 = mybir.dt.bfloat16
I32 = mybir.dt.int32

KEEP_SHARE = 4
STRUCK = -1e30
LN_EPS = 1e-5
NORM_FLOOR = 1e-12

BQ, BK, BV, BG, BO, BVX, BF = range(7)


def at(batch, per_batch, n):
    return batch * per_batch + n


class Steps:

    def __init__(self, engine, sem):
        self.engine, self.sem, self.n = engine, sem, 0

    def mark(self, instruction):
        instruction.then_inc(self.sem, 1)
        self.n += 1
        return self.n

    def wait(self, n):
        self.engine.wait_ge(self.sem, n)

    def restart(self):
        if self.n:
            self.engine.wait_ge(self.sem, self.n)
            self.engine.sem_clear(self.sem)
        self.n = 0


def decoder_layer(nc, x, ctx, aWq, abq, aWk, abk, aWv, abv, aWo, abo, aWt, abt, aWg, abg,
                  xWq, xbq, xWk, xbk, xWv, xbv, fW, fb, fids, fweights, out):
    B, S, D = x.shape
    C = ctx.shape[2]
    H, DH = 16, D // 16
    NT = S // P
    KD, KC = D // P, C // P
    HQ = P // DH
    NQ = NT * (H // HQ)
    G = H // HQ
    ROUNDS = S // KEEP_SHARE // 8
    NW = fids.shape[0]
    assert NT == 2 and KD == 4 and KC == 2 and NQ == 8 and S == 256

    stack = ExitStack()
    with stack:
        def sb(name, shape, dt=F32):
            return stack.enter_context(nc.sbuf_tensor(name, shape, dt))

        def sem(name):
            return stack.enter_context(nc.semaphore(name))

        w_q, w_k, w_v, w_g, w_o = (sb(n, [P, KD, D]) for n in ("w_q", "w_k", "w_v", "w_g", "w_o"))
        w_a = sb("w_a", [P, KD, C])
        w_vx = sb("w_vx", [P, KC, D])
        w_f = sb("w_f", [P, KD, D])
        wt_cols = sb("wt_cols", [P, KD])
        wt_wide = sb("wt_wide", [P, KD, P])
        neg_bt = sb("neg_bt", [P, 1])
        b_a = sb("b_a", [P, KC])
        bq_cols = sb("bq_cols", [P, KD])
        bias_rows = sb("bias_rows", [3, 7, D], BF16)
        ones_rows = sb("ones_rows", [3, P], BF16)
        ident = sb("ident", [P, P])
        ones = sb("ones", [P, P])
        f_w_wide = sb("f_w_wide", [P, NW])
        f_w_col = sb("f_w_col", [NW, 1])
        f_w_cols = sb("f_w_cols", [NW, 3])
        f_b_rows = sb("f_b_rows", [NW, D])
        ids_sb = sb("ids_sb", [1, NW], I32)
        minus_half = sb("minus_half", [P, 2 * H * NT])

        x_in = sb("x_in", [P, NT, D])
        x_res = sb("x_res", [P, NT, D])
        xT = sb("xT", [P, KD, S])
        qk = sb("qk", [P, NT, 2 * D])
        sq = sb("sq", [P, NT, 2 * D])
        sumsq = sb("sumsq", [P, NT, 2 * H])
        inv_norm = sb("inv_norm", [P, NT, 2 * H])
        t_scratch = sb("t_scratch", [P, S])
        t_small = sb("t_small", [P, 6])
        qT = sb("qT", [P, HQ, G, S])
        kT = sb("kT", [P, G, S])
        v_sb = sb("v_sb", [P, NT, D])
        gate_e = sb("gate_e", [P, NT, D])
        attnT = sb("attnT", [P, G, S])
        scores = sb("scores", [P, 2, HQ, S])
        probs = sb("probs", [P, 4, HQ, S])
        probsT = sb("probsT", [P, 2, HQ, NT, P])
        top8 = sb("top8", [P, HQ, 8])
        inv_sum = sb("inv_sum", [P, P])
        after_cross = sb("after_cross", [P, 2, NT * D])
        y, x3 = (after_cross[:, n].rearrange("p (t d) -> p t d", t=NT) for n in range(2))
        mix = sb("mix", [P, D])
        stats = sb("stats", [P, NT, 6])
        mean_var = sb("mean_var", [P, NT, 2])
        rstd = sb("rstd", [P, NT])
        shift = sb("shift", [P, NT])
        normed = sb("normed", [P, 4, NT * D])
        x1, x2 = (normed[:, n].rearrange("p (t d) -> p t d", t=NT) for n in (0, 2))
        x1T, x2T = (normed[:, n].rearrange("p (a k) -> p a k", a=KD) for n in (1, 3))
        aT = sb("aT", [P, KC, S])
        c_sb = sb("c_sb", [P, NT, C])
        cT = sb("cT", [P, KC, S])
        neg_max = sb("neg_max", [P, NT])
        x_sum = sb("x_sum", [P, NT])
        x_inv = sb("x_inv", [P, NT])
        p2 = sb("p2", [P, NT, S])
        p2T = sb("p2T", [P, NT, NT, P])
        pcT = sb("pcT", [P, KC, S])

        raw_wq = probs[:, 0:2].rearrange("p a h k -> p (a h k)").rearrange("p (a n) -> p a n", a=KD)
        raw_wk = probs[:, 2].rearrange("p h k -> p (h k)").rearrange("p (a n) -> p a n", a=KC)
        wqT = qk[:].rearrange("p t n -> p (t n)").rearrange("p (a n) -> p a n", a=KD)
        wkT = attnT
        f_stage = [scores[:].rearrange("p a h k -> p (a h k)"), sq[:].rearrange("p t n -> p (t n)")]
        bias_f32 = normed[0:3].rearrange("p a n -> p (a n)")[:, 0:7 * D].rearrange("p (a n) -> p a n", a=7)
        bias_part = after_cross[0:3].rearrange("p a n -> p (a n)")[:, 0:7 * D // 2].bitcast(BF16)\
            .rearrange("p (a n) -> p a n", a=7)
        f_sum = probsT[:].rearrange("p a h k n -> p (a h k n)")

        score_ps = stack.enter_context(nc.psum_tensor("score_ps", [P, 2, HQ, S], F32))
        T = [stack.enter_context(nc.psum_tensor(f"turn_ps{i}", [P, 512], F32)) for i in range(2)]
        A = [stack.enter_context(nc.psum_tensor(f"acc_ps{i}", [P, 512], F32)) for i in range(2)]

        s_wload = sem("weights_loaded")
        s_small = sem("small_loaded")
        s_rawx = sem("raw_cross_weights_loaded")
        s_ids = sem("ids_loaded")
        s_fload = [sem(f"adapter_loaded{i}") for i in range(2)]
        s_fused = sem("adapter_added")
        s_const = sem("constants_made")
        s_const0 = sem("identity_zeroed")
        s_fill = sem("setup_filled")
        s_empty = sem("setup_emptied")
        s_bias = sem("bias_rows_ready")
        s_wide = sem("wide_weights_ready")
        s_x = sem("x_loaded")
        s_res = sem("x_res_loaded")
        s_c = sem("ctx_loaded")
        s_xt_f = sem("x_turned")
        s_tmp_f = sem("temp_product")
        s_qk_f = sem("qk_product")
        s_qkt_f = sem("qk_turned")
        s_sc_f = sem("scores_product")
        s_v_f = sem("v_product")
        s_g_f = sem("gate_product")
        s_pt_f = sem("probs_turned")
        s_pv_f = sem("attn_product")
        s_o_f = sem("out_product")
        s_x1t_f = sem("x1_turned")
        s_a_f = sem("a_product")
        s_ct_f = sem("ctx_turned")
        s_s2_f = sem("cross_scores_product")
        s_p2t_f = sem("cross_probs_turned")
        s_pc_f = sem("cross_context_product")
        s_xv_f = sem("cross_value_product")
        s_x2t_f = sem("x2_turned")
        s_f_f = sem("ffn_product")
        s_xt = sem("xT_ready")
        s_tmp = sem("mean_logit_ready")
        s_te = sem("temp_exp_ready")
        s_qk = sem("qk_copied")
        s_sq = sem("squares_ready")
        s_ss = sem("sumsq_ready")
        s_in = sem("inv_norm_ready")
        s_tn = sem("temp_folded")
        s_qn = sem("qk_normalised")
        s_qkt = sem("qkT_ready")
        s_sc = sem("scores_copied")
        s_ex = sem("exps_ready")
        s_pr = sem("probs_ready")
        s_pt = sem("probsT_ready")
        s_at = sem("attnT_ready")
        s_v = sem("v_copied")
        s_g = sem("gate_exp_ready")
        s_mix = sem("out_taken")
        s_y1 = sem("stats1_ready")
        s_x1 = sem("x1_ready")
        s_x1t = sem("x1T_ready")
        s_a = sem("aT_ready")
        s_ct = sem("cT_ready")
        s_mx = sem("cross_max_ready")
        s_p2 = sem("cross_exp_ready")
        s_p2n = sem("cross_probs_ready")
        s_p2t = sem("p2T_ready")
        s_pc = sem("pcT_ready")
        s_y2 = sem("cross_taken")
        s_y2s = sem("stats2_ready")
        s_x2 = sem("x2_ready")
        s_x2t = sem("x2T_ready")
        s_y3 = sem("ffn_taken")
        s_y3s = sem("stats3_ready")
        s_x3 = sem("x3_ready")
        s_out = sem("out_stored")
        s_dve = sem("vector_step")
        s_pool = sem("pool_step")
        s_seq = sem("wait_carriers")

        x_v = x.rearrange("b (t p) d -> b p t d", p=P)
        c_v = ctx.rearrange("b (t p) d -> b p t d", p=P)
        o_v = out.rearrange("b (t p) d -> b p t d", p=P)

        def of(view, b):
            if isinstance(b, int):
                return view[b]
            return view[bass.ds(b, 1)].rearrange("u p t d -> (u p) t d")

        block = stack.enter_context(nc.Block())

        @block.sync
        def _(sp):
            def load_x(b):
                if not isinstance(b, int) or b:
                    sp.wait_ge(s_xt_f, at(b, NT, 0))
                sp.dma_start(x_in[:], of(x_v, b)).then_inc(s_x, 16)

            def load_for_back(b):
                if not isinstance(b, int) or b:
                    sp.wait_ge(s_y1, at(b, NT, 0))
                    sp.wait_ge(s_pc_f, at(b, 1, 0))
                sp.dma_start(x_res[:], of(x_v, b)).then_inc(s_res, 16)
                sp.dma_start(c_sb[:], of(c_v, b)).then_inc(s_c, 16)

            def store(b):
                sp.wait_ge(s_x3, at(b, NT, NT))
                sp.dma_start(of(o_v, b), x3).then_inc(s_out, 16)

            def setup():
                sp.dma_start(x_in[:], of(x_v, 0)).then_inc(s_x, 16)
                sp.dma_start(ids_sb[:], fids.rearrange("(a k) -> a k", a=1)).then_inc(s_ids, 16)
                sp.dma_start(raw_wq, xWq.rearrange("(a p) n -> p a n", p=P)).then_inc(s_rawx, 16)
                sp.dma_start(raw_wk, xWk.rearrange("(a p) n -> p a n", p=P)).then_inc(s_rawx, 16)
                sp.dma_start(f_w_wide[:], fweights.partition_broadcast(P)).then_inc(s_small, 16)
                sp.dma_start(f_w_col[:], fweights.rearrange("(k a) -> k a", a=1)).then_inc(s_small, 16)
                for n, b in enumerate((abq, abk, abv, abg, abo, xbv)):
                    sp.dma_start(bias_f32[:, n], b.partition_broadcast(3)).then_inc(s_small, 16)
                with nc.allow_non_contiguous_dma(reason="three short vectors, once"):
                    sp.dma_start(wt_cols[:], aWt.rearrange("(a p) n -> p (a n)", p=P)).then_inc(s_small, 16)
                    sp.dma_start(bq_cols[:], xbq.rearrange("(a p) -> p a", p=P)).then_inc(s_small, 16)
                sp.dma_start(neg_bt[:], abt.partition_broadcast(P)).then_inc(s_small, 16)
                sp.wait_ge(s_ids, 16)
                fW_v = fW.rearrange("n (a p) d -> n p a d", p=P)
                ids = [sp.value_load(ids_sb[0:1, k:k + 1], min_val=0, max_val=fW.shape[0] - 1) for k in range(NW)]
                for k, n in enumerate(ids):
                    sp.dma_start(f_b_rows[k:k + 1], fb[bass.ds(n, 1)]).then_inc(s_small, 16)
                for k, n in enumerate(ids):
                    if k >= 2:
                        sp.wait_ge(s_fused, k - 1)
                    sp.dma_start(f_stage[k % 2].rearrange("p (a d) -> p a d", a=KD),
                                 fW_v[bass.ds(n, 1)].rearrange("u p a d -> (u p) a d"))\
                      .then_inc(s_fload[k % 2], 16)

            setup()
            load_for_back(0)
            load_x(1)
            with sp.Fori(1, B - 1) as i:
                load_x(i + 1)
                load_for_back(i)
                store(i - 1)
            load_for_back(B - 1)
            store(B - 2)
            store(B - 1)
            sp.wait_ge(s_out, 16 * B)

        @block.gpsimd
        def _(pool):
            step = Steps(pool, s_pool)

            def setup():
                for w, src in ((w_q, aWq), (w_k, aWk), (w_v, aWv), (w_g, aWg), (w_o, aWo), (w_vx, xWv)):
                    pool.dma_start(w[:], src.rearrange("(a p) n -> p a n", p=P)).then_inc(s_wload, 16)
                pool.memset(ident[:], 0.0).then_inc(s_const0, 1)
                pool.memset(ones[:], 1.0).then_inc(s_const, 1)
                pool.memset(ones_rows[:], 1.0).then_inc(s_const, 1)
                pool.memset(minus_half[:], -0.5).then_inc(s_const, 1)
                pool.memset(qT[:], 0.0).then_inc(s_const, 1)
                pool.wait_ge(s_const0, 1)
                pool.affine_select(out=ident[:], in_=ident[:], compare_op=ALU.not_equal, fill=1.0,
                                   base=0, pattern=[[-1, P]], channel_multiplier=1).then_inc(s_const, 1)
                pool.wait_ge(s_const, 5)

            def squares(b):
                for n in range(2 * NT):
                    t, half = divmod(n, 2)
                    part = slice(half * D, half * D + D)
                    pool.wait_ge(s_qk, at(b, 2 * NT, n + 1))
                    pool.tensor_tensor(sq[:, t, part], qk[:, t, part], qk[:, t, part], ALU.mult)\
                        .then_inc(s_sq, 1)

            def norms(b):
                pool.wait_ge(s_ss, at(b, 1, 1))
                pool.sem_inc(s_seq, 1)
                step.wait(step.mark(pool.tensor_scalar(sumsq[:], sumsq[:], NORM_FLOOR ** 2, None, ALU.max)))
                pool.tensor_tensor(inv_norm[:].rearrange("p t h -> p (t h)"), sumsq[:].rearrange("p t h -> p (t h)"),
                                   minus_half[:], ALU.pow).then_inc(s_in, 1)
                pool.wait_ge(s_tn, at(b, 1, 1))
                for t in range(NT):
                    v = qk[:, t].rearrange("p (h d) -> p h d", d=DH)
                    pool.tensor_tensor(v, v, inv_norm[:, t].unsqueeze(2).to_broadcast([P, 2 * H, DH]), ALU.mult)\
                        .then_inc(s_qn, 1)

            def layernorm(b, stats_sem, dst, dst_sem, src, store_wait=None):
                if store_wait is not None:
                    pool.wait_ge(s_out, store_wait)
                pool.wait_ge(stats_sem, at(b, NT, NT))
                pool.sem_inc(s_seq, 1)
                step.wait(step.mark(pool.tensor_scalar(rstd[:], mean_var[:, :, 1], LN_EPS, None, ALU.add)))
                step.wait(step.mark(pool.tensor_tensor(rstd[:], rstd[:], minus_half[:, 0:NT], ALU.pow)))
                step.wait(step.mark(pool.tensor_tensor(shift[:], mean_var[:, :, 0], rstd[:], ALU.mult)))
                step.wait(step.mark(pool.tensor_scalar(shift[:], shift[:], -1.0, None, ALU.mult)))
                for t in range(NT):
                    pool.tensor_scalar(dst[:, t], src[:, t], rstd[:, t:t + 1], shift[:, t:t + 1],
                                       ALU.mult, ALU.add).then_inc(dst_sem, 1)

            def body(i, first, last):
                step.restart()
                if not first:
                    layernorm(i - 1, s_y1, x1, s_x1, y)
                    layernorm(i - 1, s_y2s, x2, s_x2, y)
                    layernorm(i - 1, s_y3s, x3, s_x3, y, at(i - 1, 16, 0))
                if not last:
                    squares(i + 1)
                    norms(i + 1)

            setup()
            squares(0)
            norms(0)
            body(0, True, False)
            with pool.Fori(1, B - 1) as i:
                body(i, False, False)
            body(B - 1, False, True)
            step.restart()
            layernorm(B - 1, s_y1, x1, s_x1, y)
            layernorm(B - 1, s_y2s, x2, s_x2, y)
            layernorm(B - 1, s_y3s, x3, s_x3, y, 16 * (B - 1))

        @block.scalar
        def _(act):
            def setup():
                n = 0
                for et in range(KD):
                    n += 1
                    act.wait_ge(s_fill, n)
                    act.activation(wqT[:, et], T[n % 2][:], ACT.Copy).then_inc(s_empty, 1)
                for e2 in range(KD // 2):
                    n += 1
                    act.wait_ge(s_fill, n)
                    act.activation(wkT[:, 2 * e2:2 * e2 + 2], T[n % 2][:].rearrange("p (a c) -> p a c", a=2),
                                   ACT.Copy).then_inc(s_empty, 1)
                for dt in range(KD):
                    n += 1
                    act.wait_ge(s_fill, n)
                    act.activation(w_a[:, dt], A[dt % 2][:, 0:C], ACT.Copy).then_inc(s_empty, 1)
                n += 1
                act.wait_ge(s_fill, n)
                act.activation(b_a[:], A[0][:, 0:KC], ACT.Copy).then_inc(s_empty, 1)
                n += 1
                act.wait_ge(s_fill, n)
                act.activation(bias_f32[:, BF], A[1][0:3, :], ACT.Copy).then_inc(s_empty, 1)
                for dt in range(KD):
                    n += 1
                    act.wait_ge(s_fill, n)
                    act.activation(w_f[:, dt], T[n % 2][:], ACT.Copy).then_inc(s_empty, 1)
                act.wait_ge(s_small, 16 * (11 + NW))
                act.activation(neg_bt[:], neg_bt[:], ACT.Copy, scale=-1.0).then_inc(s_empty, 1)
                act.wait_ge(s_empty, n + 1)

            def front_x(b):
                for t in range(NT):
                    act.wait_ge(s_xt_f, at(b, NT, t + 1))
                    act.activation(xT[:, :, t * P:t * P + P], T[t][:].rearrange("p (a k) -> p a k", a=KD),
                                   ACT.Copy).then_inc(s_xt, 1)

            def front_qk(b):
                act.wait_ge(s_tmp_f, at(b, 1, 1))
                act.activation(t_scratch[:], A[0][:, 0:S], ACT.Identity, scale=1.0 / S,
                               accum_out=t_small[:, 0:1]).then_inc(s_tmp, 1)
                for t in range(NT):
                    for half in range(2):
                        act.wait_ge(s_qk_f, at(b, 2 * NT, 2 * t + half + 1))
                        act.activation(qk[:, t, half * D:half * D + D], A[1 - half][:], ACT.Copy).then_inc(s_qk, 1)
                    if t == 0:
                        act.wait_ge(s_tmp, at(b, 1, 1))
                        act.activation(t_small[:, 1:2], t_small[:, 0:1], ACT.Exp, scale=-1.0,
                                       bias=neg_bt[:]).then_inc(s_te, 1)

            def front_turn(b):
                for t in range(NT):
                    part = slice(t * P, t * P + P)
                    act.wait_ge(s_qkt_f, at(b, 2 * NT, 2 * t + 1))
                    for j in range(HQ):
                        rows = slice(j * DH, j * DH + DH)
                        last = act.activation(qT[rows, j, :, part], T[0][rows].rearrange("p (g k) -> p g k", g=G),
                                              ACT.Copy)
                    last.then_inc(s_qkt, 1)
                    act.wait_ge(s_qkt_f, at(b, 2 * NT, 2 * t + 2))
                    act.activation(kT[:, :, part], T[1][:].rearrange("p (g k) -> p g k", g=G), ACT.Copy)\
                       .then_inc(s_qkt, 1)

            def take_scores(b, s):
                act.wait_ge(s_sc_f, at(b, NQ, s + 1))
                if s >= 2:
                    act.wait_ge(s_pr, at(b, NQ, s - 1))
                elif not (isinstance(b, int) and b == 0):
                    act.wait_ge(s_pr, at(b - 1, NQ, NQ + s - 1))
                act.activation(scores[:, s % 2], score_ps[:, s % 2], ACT.Copy).then_inc(s_sc, 1)
                if s >= 4:
                    act.wait_ge(s_pt_f, at(b, 2 * NQ, 2 * (s - 3)))
                elif not (isinstance(b, int) and b == 0):
                    act.wait_ge(s_pt_f, at(b - 1, 2 * NQ, 2 * (NQ + s - 3)))
                act.activation(probs[:, s % 4], score_ps[:, s % 2], ACT.Exp).then_inc(s_ex, 1)

            def take_probs(b, s):
                for half in range(2):
                    act.wait_ge(s_pt_f, at(b, 2 * NQ, 2 * s + half + 1))
                    if half == 0 and s >= 2:
                        act.wait_ge(s_pv_f, at(b, NQ, s - 1))
                    act.activation(probsT[:, s % 2, 2 * half:2 * half + 2],
                                   T[half][:].rearrange("p (h k n) -> p h k n", h=2, k=NT), ACT.Copy)\
                       .then_inc(s_pt, 1)

            def values(b):
                for t in range(NT):
                    act.wait_ge(s_v_f, at(b, NT, t + 1))
                    act.activation(v_sb[:, t], A[1 - t][:], ACT.Copy).then_inc(s_v, 1)

            def gates(b):
                for t in range(NT):
                    act.wait_ge(s_g_f, at(b, NT, t + 1))
                    act.activation(gate_e[:, t], A[1 - t][:], ACT.Exp, scale=-1.0).then_inc(s_g, 1)

            def turn_tiles(b, filled, dst, ready):
                for t in range(NT):
                    act.wait_ge(filled, at(b, NT, t + 1))
                    act.activation(dst[:, :, t * P:t * P + P], T[t][:].rearrange("p (a k) -> p a k", a=KD),
                                   ACT.Copy).then_inc(ready, 1)

            def cross_front(b):
                turn_tiles(b, s_x1t_f, x1T, s_x1t)
                for c in range(KC):
                    act.wait_ge(s_a_f, at(b, KC, c + 1))
                    act.activation(aT[:, c], A[c][:, 0:S], ACT.Identity, bias=b_a[:, c:c + 1]).then_inc(s_a, 1)
                act.wait_ge(s_ct_f, at(b, 1, 1))
                act.activation(cT[:], T[0][:].rearrange("p (c k) -> p c k", c=KC), ACT.Copy).then_inc(s_ct, 1)

            def cross_exp(b):
                for t in range(NT):
                    act.wait_ge(s_mx, at(b, NT, t + 1))
                    act.activation(p2[:, t], A[1 - t][:, 0:S], ACT.Exp, bias=neg_max[:, t:t + 1],
                                   accum_out=x_sum[:, t:t + 1]).then_inc(s_p2, 1)

            def cross_back(b):
                act.wait_ge(s_p2t_f, at(b, 1, 1))
                act.activation(p2T[:], T[0][:].rearrange("p (t k n) -> p t k n", t=NT, k=NT), ACT.Copy)\
                   .then_inc(s_p2t, 1)
                act.wait_ge(s_pc_f, at(b, 1, 1))
                act.activation(pcT[:], A[1][:].rearrange("p (c k) -> p c k", c=KC), ACT.Copy).then_inc(s_pc, 1)

            def body(i, first, last):
                if not first:
                    take_probs(i - 1, NQ - 1)
                values(i)
                take_scores(i, 1)
                for s in range(1, NQ):
                    take_probs(i, s - 1)
                    if not first and s == 2:
                        cross_front(i - 1)
                        cross_exp(i - 1)
                    if not first and s == 3:
                        cross_back(i - 1)
                    if s == 3:
                        gates(i)
                    if not first and s == 4:
                        turn_tiles(i - 1, s_x2t_f, x2T, s_x2t)
                    if not last and s == 4:
                        front_x(i + 1)
                    if s < NQ - 1:
                        take_scores(i, s + 1)
                    if not last and s == 5:
                        front_qk(i + 1)
                if not last:
                    front_turn(i + 1)
                    take_scores(i + 1, 0)

            setup()
            front_x(0)
            front_qk(0)
            front_turn(0)
            take_scores(0, 0)
            body(0, True, False)
            with act.Fori(1, B - 1) as i:
                body(i, False, False)
            body(B - 1, False, True)
            take_probs(B - 1, NQ - 1)
            cross_front(B - 1)
            cross_exp(B - 1)
            cross_back(B - 1)
            turn_tiles(B - 1, s_x2t_f, x2T, s_x2t)

        @block.tensor
        def _(pe):
            def turn(dst, parts):
                for n, part in enumerate(parts):
                    last = pe.transpose(dst[:, n * P:n * P + P], part, ident[:])
                return last

            def add_bias(dst, n):
                return pe.matmul(dst, ones_rows[:], bias_rows[:, n], start=False, stop=True)

            def setup():
                pe.wait_ge(s_const, 5)
                pe.wait_ge(s_rawx, 32)
                n = 0
                for et in range(KD):
                    n += 1
                    if n > 2:
                        pe.wait_ge(s_empty, n - 2)
                    turn(T[n % 2], [raw_wq[:, dt, et * P:et * P + P] for dt in range(KD)]).then_inc(s_fill, 1)
                for e2 in range(KD // 2):
                    n += 1
                    pe.wait_ge(s_empty, n - 2)
                    turn(T[n % 2], [raw_wk[:, ct, et * P:et * P + P] for et in (2 * e2, 2 * e2 + 1)
                                    for ct in range(KC)]).then_inc(s_fill, 1)
                pe.wait_ge(s_empty, n)
                for dt in range(KD):
                    n += 1
                    if dt >= 2:
                        pe.wait_ge(s_empty, n - 2)
                    for et in range(KD):
                        mm = pe.matmul(A[dt % 2][:, 0:C], wqT[:, et, dt * P:dt * P + P], wkT[:, et],
                                       start=et == 0, stop=et == KD - 1)
                    mm.then_inc(s_fill, 1)
                pe.wait_ge(s_small, 16 * (11 + NW))
                n += 1
                pe.wait_ge(s_empty, n - 1)
                for ct in range(KC):
                    for et in range(KD):
                        mm = pe.matmul(A[0][:, ct:ct + 1], wkT[:, et, ct * P:ct * P + P], bq_cols[:, et:et + 1],
                                       start=et == 0, stop=et == KD - 1)
                mm.then_inc(s_fill, 1)
                n += 1
                pe.wait_ge(s_wide, 1)
                pe.matmul(A[1][0:3, :], f_w_cols[:], f_b_rows[:], start=True, stop=True).then_inc(s_fill, 1)
                pe.wait_ge(s_fused, NW)
                pe.wait_ge(s_empty, n)
                for dt in range(KD):
                    n += 1
                    if dt >= 2:
                        pe.wait_ge(s_empty, n - 2)
                    turn(T[n % 2], [f_sum[:, ot * D + dt * P:ot * D + dt * P + P] for ot in range(KD)])\
                        .then_inc(s_fill, 1)
                pe.wait_ge(s_empty, n + 1)
                pe.wait_ge(s_bias, 1)
                pe.wait_ge(s_wload, 16 * 6)

            def project(dst, src, w, bias, t, kts=KD):
                for kt in range(kts):
                    pe.matmul(dst, src[:, kt, t * P:t * P + P], w[:, kt], start=kt == 0, stop=False)
                return add_bias(dst, bias)

            def front_x(b):
                pe.wait_ge(s_x, at(b, 16, 16))
                for t in range(NT):
                    turn(T[t], [x_in[:, t, kt * P:kt * P + P] for kt in range(KD)]).then_inc(s_xt_f, 1)

            def front_temp(b):
                pe.wait_ge(s_xt, at(b, NT, NT))
                for kt in range(KD):
                    mm = pe.matmul(A[0][:, 0:S], wt_wide[:, kt], xT[:, kt], start=kt == 0, stop=kt == KD - 1)
                mm.then_inc(s_tmp_f, 1)

            def front_qk(b):
                for t in range(NT):
                    for half, (w, bias) in enumerate(((w_q, BQ), (w_k, BK))):
                        if t == 0 and half == 1:
                            pe.wait_ge(s_tmp, at(b, 1, 1))
                        if t == 1:
                            pe.wait_ge(s_qk, at(b, 2 * NT, half + 1))
                        project(A[1 - half][:], xT, w, bias, t).then_inc(s_qk_f, 1)

            def front_turn(b):
                for t in range(NT):
                    pe.wait_ge(s_qn, at(b, NT, t + 1))
                    for half in range(2):
                        if t == 1:
                            pe.wait_ge(s_qkt, at(b, 2 * NT, half + 1))
                        turn(T[half], [qk[:, t, half * D + g * P:half * D + g * P + P] for g in range(G)])\
                            .then_inc(s_qkt_f, 1)

            def make_scores(b, s):
                t, g = divmod(s, G)
                if s >= 2:
                    pe.wait_ge(s_ex, at(b, NQ, s - 1))
                elif not (isinstance(b, int) and b == 0):
                    pe.wait_ge(s_ex, at(b - 1, NQ, NQ + s - 1))
                if s == 0:
                    pe.wait_ge(s_qkt, at(b, 2 * NT, 2 * NT))
                for j in range(HQ):
                    mm = pe.matmul(score_ps[:, s % 2, j], qT[:, j, g, t * P:t * P + P], kT[:, g],
                                   start=True, stop=True)
                mm.then_inc(s_sc_f, 1)

            def turn_probs(b, s):
                pe.wait_ge(s_pr, at(b, NQ, s + 1))
                for half in range(2):
                    turn(T[half], [probs[:, s % 4, h, kh * P:kh * P + P] for h in (2 * half, 2 * half + 1)
                                   for kh in range(NT)]).then_inc(s_pt_f, 1)

            def attend(b, s, bank):
                t, g = divmod(s, G)
                pe.wait_ge(s_pt, at(b, 2 * NQ, 2 * s + 2))
                for part in range(2):
                    for j in range(HQ):
                        h = g * HQ + j
                        for kh in range(NT):
                            w = v_sb[:, kh, h * DH:h * DH + DH] if part == 0 else ones[:, 0:DH]
                            mm = pe.matmul(A[bank][j * DH:j * DH + DH, part * P:part * P + P], w,
                                           probsT[:, s % 2, j, kh], start=kh == 0, stop=kh == NT - 1)
                mm.then_inc(s_pv_f, 1)

            def body(i, first, last):
                prev = i - 1
                if not first:
                    turn_probs(prev, NQ - 1)
                    pe.wait_ge(s_at, at(prev, NQ, NQ - 1))
                    attend(prev, NQ - 1, 0)
                if first:
                    pe.wait_ge(s_qk, at(0, 2 * NT, 2 * NT))
                for t in range(NT):
                    if t == 1 and not first:
                        pe.wait_ge(s_at, at(prev, NQ, NQ))
                    project(A[1 - t][:], xT, w_v, BV, t).then_inc(s_v_f, 1)
                make_scores(i, 1)
                turn_probs(i, 0)
                pe.wait_ge(s_v, at(i, NT, NT))
                attend(i, 0, 1)
                if not first:
                    pe.wait_ge(s_at, at(prev, NQ, NQ))
                    project(A[0][:], attnT, w_o, BO, 0).then_inc(s_o_f, 1)
                    pe.wait_ge(s_at, at(i, NQ, 1))
                    project(A[1][:], attnT, w_o, BO, 1).then_inc(s_o_f, 1)
                make_scores(i, 2)
                turn_probs(i, 1)
                if not first:
                    pe.wait_ge(s_mix, at(prev, NT, 1))
                attend(i, 1, 0)
                if not first:
                    cross_front(i, prev)
                make_scores(i, 3)
                turn_probs(i, 2)
                pe.wait_ge(s_at, at(i, NQ, 2))
                if not first:
                    pe.wait_ge(s_p2, at(prev, NT, NT))
                attend(i, 2, 0)
                if not first:
                    cross_back(i, prev)
                    pe.wait_ge(s_y2, at(prev, NT, NT))
                else:
                    pe.wait_ge(s_at, at(i, NQ, 3))
                for t in range(NT):
                    project(A[1 - t][:], xT, w_g, BG, t).then_inc(s_g_f, 1)
                make_scores(i, 4)
                turn_probs(i, 3)
                pe.wait_ge(s_g, at(i, NT, 2))
                attend(i, 3, 0)
                if not first:
                    ffn(i, prev)
                if not last:
                    pe.wait_ge(s_pt, at(i, 2 * NQ, 8))
                    if not first:
                        pe.wait_ge(s_x2t, at(prev, NT, NT))
                    front_x(i + 1)
                make_scores(i, 5)
                if not last:
                    pe.wait_ge(s_xt, at(i + 1, NT, NT))
                turn_probs(i, 4)
                if not first:
                    pe.wait_ge(s_y3, at(prev, NT, 1))
                attend(i, 4, 1)
                if not last:
                    if first:
                        pe.wait_ge(s_at, at(i, NQ, 4))
                    else:
                        pe.wait_ge(s_y3, at(prev, NT, 2))
                    front_temp(i + 1)
                make_scores(i, 6)
                if not last:
                    pe.wait_ge(s_at, at(i, NQ, 5))
                    front_qk(i + 1)
                turn_probs(i, 5)
                if not last:
                    pe.wait_ge(s_qk, at(i + 1, 2 * NT, 2 * NT))
                else:
                    pe.wait_ge(s_at, at(i, NQ, 5))
                attend(i, 5, 1)
                make_scores(i, 7)
                turn_probs(i, 6)
                if last:
                    pe.wait_ge(s_y3, at(prev, NT, 2))
                attend(i, 6, 0)
                if not last:
                    pe.wait_ge(s_pt, at(i, 2 * NQ, 14))
                    front_turn(i + 1)
                    make_scores(i + 1, 0)

            def cross_front(i, b):
                pe.wait_ge(s_x1, at(b, NT, NT))
                for t in range(NT):
                    if i is not None:
                        pe.wait_ge(s_pt, at(i, 2 * NQ, 3 + t))
                    turn(T[t], [x1[:, t, kt * P:kt * P + P] for kt in range(KD)]).then_inc(s_x1t_f, 1)
                pe.wait_ge(s_x1t, at(b, NT, NT))
                for c in range(KC):
                    if c == 0 and i is not None:
                        pe.wait_ge(s_at, at(i, NQ, 2))
                    if c == 1:
                        pe.wait_ge(s_mix, at(b, NT, 2))
                    for kt in range(KD):
                        mm = pe.matmul(A[c][:, 0:S], w_a[:, kt, c * P:c * P + P], x1T[:, kt],
                                       start=kt == 0, stop=kt == KD - 1)
                    mm.then_inc(s_a_f, 1)
                pe.wait_ge(s_c, at(b, 16, 16))
                turn(T[0], [c_sb[:, t, c * P:c * P + P] for c in range(KC) for t in range(NT)])\
                    .then_inc(s_ct_f, 1)
                pe.wait_ge(s_ct, at(b, 1, 1))
                pe.wait_ge(s_a, at(b, KC, KC))
                for t in range(NT):
                    for c in range(KC):
                        mm = pe.matmul(A[1 - t][:, 0:S], aT[:, c, t * P:t * P + P], cT[:, c],
                                       start=c == 0, stop=c == KC - 1)
                    mm.then_inc(s_s2_f, 1)

            def cross_back(i, b):
                pe.wait_ge(s_p2n, at(b, NT, NT))
                if i is not None:
                    pe.wait_ge(s_pt, at(i, 2 * NQ, 6))
                turn(T[0], [p2[:, t, kh * P:kh * P + P] for t in range(NT) for kh in range(NT)])\
                    .then_inc(s_p2t_f, 1)
                pe.wait_ge(s_p2t, at(b, 1, 1))
                for c in range(KC):
                    for kh in range(NT):
                        mm = pe.matmul(A[1][:, c * S:c * S + S], c_sb[:, kh, c * P:c * P + P], p2T[:, :, kh],
                                       start=kh == 0, stop=kh == NT - 1)
                mm.then_inc(s_pc_f, 1)
                pe.wait_ge(s_pc, at(b, 1, 1))
                if i is not None:
                    pe.wait_ge(s_at, at(i, NQ, 3))
                for t in range(NT):
                    project(A[t][:], pcT, w_vx, BVX, t, KC).then_inc(s_xv_f, 1)

            def ffn(i, b):
                pe.wait_ge(s_x2, at(b, NT, NT))
                for t in range(NT):
                    if i is not None:
                        pe.wait_ge(s_pt, at(i, 2 * NQ, 7 + t))
                    turn(T[t], [x2[:, t, kt * P:kt * P + P] for kt in range(KD)]).then_inc(s_x2t_f, 1)
                pe.wait_ge(s_x2t, at(b, NT, NT))
                pe.wait_ge(s_y2, at(b, NT, 2))
                project(A[1][:], x2T, w_f, BF, 0).then_inc(s_f_f, 1)
                if i is not None:
                    pe.wait_ge(s_at, at(i, NQ, 4))
                project(A[0][:], x2T, w_f, BF, 1).then_inc(s_f_f, 1)

            setup()
            front_x(0)
            front_temp(0)
            front_qk(0)
            front_turn(0)
            make_scores(0, 0)
            body(0, True, False)
            with pe.Fori(1, B - 1) as i:
                body(i, False, False)
            body(B - 1, False, True)
            turn_probs(B - 1, NQ - 1)
            pe.wait_ge(s_at, at(B - 1, NQ, NQ - 1))
            attend(B - 1, NQ - 1, 0)
            pe.wait_ge(s_at, at(B - 1, NQ, NQ))
            project(A[0][:], attnT, w_o, BO, 0).then_inc(s_o_f, 1)
            project(A[1][:], attnT, w_o, BO, 1).then_inc(s_o_f, 1)
            pe.wait_ge(s_mix, at(B - 1, NT, NT))
            cross_front(None, B - 1)
            cross_back(None, B - 1)
            pe.wait_ge(s_y2, at(B - 1, NT, NT))
            ffn(None, B - 1)

        @block.vector
        def _(dve):
            step = Steps(dve, s_dve)

            def setup():
                dve.wait_ge(s_const, 5)
                dve.wait_ge(s_small, 16 * (11 + NW))
                dve.tensor_scalar(f_w_cols[:], ones[0:NW, 0:3], f_w_col[:], None, ALU.mult).then_inc(s_wide, 1)
                for kt in range(KD):
                    n = step.mark(dve.tensor_scalar(wt_wide[:, kt], ones[:], wt_cols[:, kt:kt + 1], None, ALU.mult))
                for k in range(NW):
                    dve.wait_ge(s_fload[k % 2], 16 * (k // 2 + 1))
                    w = f_w_wide[:, k:k + 1]
                    if k == 0:
                        dve.tensor_scalar(f_sum, f_stage[0], w, None, ALU.mult).then_inc(s_fused, 1)
                    else:
                        dve.wait_ge(s_fused, k)
                        dve.scalar_tensor_tensor(out=f_sum, in0=f_stage[k % 2], scalar=w, in1=f_sum,
                                                 op0=ALU.mult, op1=ALU.add).then_inc(s_fused, 1)
                dve.wait_ge(s_empty, 12)
                for n in range(3):
                    m = step.mark(dve.tensor_copy(bias_part, bias_f32))
                    step.wait(m)
                    if n == 0:
                        m = step.mark(dve.tensor_scalar(bias_rows[:], bias_part, ident[0:3, 0:1], None, ALU.mult))
                    else:
                        m = step.mark(dve.scalar_tensor_tensor(
                            out=bias_rows[:], in0=bias_part, scalar=ident[0:3, n:n + 1], in1=bias_rows[:],
                            op0=ALU.mult, op1=ALU.add))
                    if n < 2:
                        m = step.mark(dve.tensor_tensor(bias_f32, bias_f32, bias_part, ALU.subtract))
                    step.wait(m)
                dve.sem_inc(s_bias, 1)

            def front_norms(b):
                dve.wait_ge(s_sq, at(b, 2 * NT, 2 * NT))
                dve.tensor_reduce(sumsq[:], sq[:].rearrange("p t (h d) -> p t h d", d=DH), AX.X, ALU.add)\
                   .then_inc(s_ss, 1)
                dve.wait_ge(s_te, at(b, 1, 1))
                step.mark(dve.tensor_scalar(t_small[:, 2:3], t_small[:, 1:2], 1.0, None, ALU.add))
                step.wait(step.mark(dve.tensor_scalar(t_small[:, 3:4], t_small[:, 1:2], 0.5, 1.5, ALU.mult, ALU.add)))
                step.wait(step.mark(dve.reciprocal(t_small[:, 4:5], t_small[:, 3:4])))
                step.wait(step.mark(dve.tensor_tensor(t_small[:, 5:6], t_small[:, 2:3], t_small[:, 4:5], ALU.mult)))
                dve.wait_ge(s_in, at(b, 1, 1))
                dve.tensor_scalar(inv_norm[:, :, 0:H], inv_norm[:, :, 0:H], t_small[:, 5:6], None, ALU.mult)\
                   .then_inc(s_tn, 1)

            def keep_top(b, s):
                dve.wait_ge(s_sc, at(b, NQ, s + 1))
                dve.sem_inc(s_seq, 1)
                struck = [0] * HQ
                for r in range(ROUNDS):
                    found = []
                    for j in range(HQ):
                        if struck[j]:
                            step.wait(struck[j])
                        found.append(step.mark(dve.max(top8[:, j], scores[:, s % 2, j])))
                    for j in range(HQ):
                        step.wait(found[j])
                        struck[j] = step.mark(dve.match_replace(scores[:, s % 2, j], top8[:, j],
                                                                scores[:, s % 2, j], STRUCK))
                step.wait(struck[-1])
                dve.wait_ge(s_ex, at(b, NQ, s + 1))
                dve.scalar_tensor_tensor(out=probs[:, s % 4], in0=scores[:, s % 2], scalar=STRUCK / 2,
                                         in1=probs[:, s % 4], op0=ALU.is_le, op1=ALU.mult).then_inc(s_pr, 1)

            def normalise(b, s, bank):
                t, g = divmod(s, G)
                dve.wait_ge(s_pv_f, at(b, NQ, s + 1))
                step.wait(step.mark(dve.reciprocal(inv_sum[:], A[bank][:, P:2 * P])))
                dve.tensor_tensor(attnT[:, g, t * P:t * P + P], A[bank][:, 0:P], inv_sum[:], ALU.mult)\
                   .then_inc(s_at, 1)

            def statistics(t, ready):
                step.wait(step.mark(dve.bn_stats(stats[:, t], y[:, t])))
                dve.bn_aggr(mean_var[:, t], stats[:, t]).then_inc(ready, 1)

            def mixing(b):
                dve.wait_ge(s_res, at(b, 16, 16))
                dve.wait_ge(s_x3, at(b, NT, 0))
                for t in range(NT):
                    step.wait(step.mark(dve.tensor_scalar(gate_e[:, t], gate_e[:, t], 1.0, None, ALU.add)))
                    step.wait(step.mark(dve.reciprocal(gate_e[:, t], gate_e[:, t])))
                    dve.wait_ge(s_o_f, at(b, NT, t + 1))
                    dve.tensor_tensor(mix[:], A[t][:], x_res[:, t], ALU.subtract).then_inc(s_mix, 1)
                    dve.wait_ge(s_mix, at(b, NT, t + 1))
                    step.wait(step.mark(dve.tensor_tensor(mix[:], mix[:], gate_e[:, t], ALU.mult)))
                    step.wait(step.mark(dve.scalar_tensor_tensor(out=y[:, t], in0=x_res[:, t], scalar=2.0,
                                                                 in1=mix[:], op0=ALU.mult, op1=ALU.add)))
                    statistics(t, s_y1)

            def cross_max(b):
                for t in range(NT):
                    dve.wait_ge(s_s2_f, at(b, NT, t + 1))
                    dve.tensor_reduce(neg_max[:, t:t + 1], A[1 - t][:, 0:S], AX.X, ALU.max, negate=True)\
                       .then_inc(s_mx, 1)

            def cross_scale(b):
                for t in range(NT):
                    dve.wait_ge(s_p2, at(b, NT, t + 1))
                    step.wait(step.mark(dve.reciprocal(x_inv[:, t:t + 1], x_sum[:, t:t + 1])))
                    dve.tensor_scalar(p2[:, t], p2[:, t], x_inv[:, t:t + 1], None, ALU.mult).then_inc(s_p2n, 1)

            def cross_add(b):
                for t in range(NT):
                    dve.wait_ge(s_xv_f, at(b, NT, t + 1))
                    dve.tensor_tensor(y[:, t], A[t][:], x1[:, t], ALU.add).then_inc(s_y2, 1)
                    dve.wait_ge(s_y2, at(b, NT, t + 1))
                    statistics(t, s_y2s)

            def ffn_add(b):
                for t in range(NT):
                    dve.wait_ge(s_f_f, at(b, NT, t + 1))
                    dve.tensor_tensor(y[:, t], A[1 - t][:], x2[:, t], ALU.add).then_inc(s_y3, 1)
                    dve.wait_ge(s_y3, at(b, NT, t + 1))
                    statistics(t, s_y3s)

            PV_BANK = [1, 0, 0, 0, 1, 1, 0, 0]

            def body(i, first, last):
                step.restart()
                prev = i - 1
                if not first:
                    normalise(prev, NQ - 1, PV_BANK[NQ - 1])
                keep_top(i, 0)
                for s in range(1, NQ):
                    keep_top(i, s)
                    if s == 1 and not first:
                        dve.wait_ge(s_o_f, at(prev, NT, 1))
                    normalise(i, s - 1, PV_BANK[s - 1])
                    if not first:
                        if s == 1:
                            mixing(prev)
                        if s == 2:
                            cross_max(prev)
                            cross_scale(prev)
                        if s == 3:
                            cross_add(prev)
                        if s == 4:
                            ffn_add(prev)
                    if s == 5 and not last:
                        front_norms(i + 1)

            setup()
            front_norms(0)
            body(0, True, False)
            step.restart()
            with dve.Fori(1, B - 1) as i:
                body(i, False, False)
                step.restart()
            body(B - 1, False, True)
            step.restart()
            normalise(B - 1, NQ - 1, 0)
            mixing(B - 1)
            cross_max(B - 1)
            cross_scale(B - 1)
            cross_add(B - 1)
            ffn_add(B - 1)


_INS = ['x', 'ctx_512', 'L0_attn_Wq', 'L0_attn_bq', 'L0_attn_Wk', 'L0_attn_bk', 'L0_attn_Wv', 'L0_attn_bv',
        'L0_attn_Wo', 'L0_attn_bo', 'L0_attn_Wt', 'L0_attn_bt', 'L0_attn_Wg', 'L0_attn_bg',
        'L0_xattn_Wq', 'L0_xattn_bq', 'L0_xattn_Wk', 'L0_xattn_bk', 'L0_xattn_Wv', 'L0_xattn_bv',
        'L0_ffn_W', 'L0_ffn_b', 'L0_ffn_ids', 'L0_ffn_weights']


def kernel(**inputs):
    import numpy as _np
    import concourse.bacc as _bacc
    from concourse import mybir as _mybir
    from concourse.bass_utils import run_bass_kernel_spmd as _run

    nc = _bacc.Bacc("TRN2", target_bir_lowering=False, num_devices=1)
    arrays, args = {}, []
    for name in _INS:
        a = _np.ascontiguousarray(inputs[name])
        arrays[f"in_{name}_dram"] = a
        args.append(nc.dram_tensor(f"in_{name}_dram", a.shape, _mybir.dt.from_np(a.dtype), kind="ExternalInput").ap())
    shape = inputs['x'].shape
    args.append(nc.dram_tensor("out_0_dram", shape, _mybir.dt.float32, kind="ExternalOutput").ap())
    decoder_layer(nc, *args)
    r = _run(nc, [arrays], core_ids=[0])
    return r.results[0]["out_0_dram"]
```
